# Optimizing a Trainium2 kernel written in Bass

```python
import numpy as np
import jax
import jax.numpy as jnp

def _softmax(x, axis=-1):
    return jax.nn.softmax(x, axis=axis)

def _gelu(x):
    return jax.nn.gelu(x, approximate=True)

def _silu(x):
    return jax.nn.silu(x)

def _sigmoid(x):
    return jax.nn.sigmoid(x)

def _layernorm(x, axis=-1, eps=1e-05):
    m = jnp.mean(x, axis=axis, keepdims=True)
    v = jnp.var(x, axis=axis, keepdims=True)
    return (x - m) / jnp.sqrt(v + eps)

def _scatter_add(tgt, idx, src, axis=0):
    return tgt.at[idx].add(src)

def _segment_sum(src, seg, n):
    return jax.ops.segment_sum(src, seg, n)
kernel_name = 'mk_seq_postln_d1_jaxref_r4_62a1d0'

def setup_inputs(seed: int=0):
    np.random.seed(seed)
    _w = jnp.asarray

    def _L0_attn_setup():
        import jax, jax.numpy as jnp
        import numpy as np
        import math
        B = 2
        D_MODEL = 512
        L_MAX = 1024
        FILTER_ORDER = 64
        EMB_DIM = 3
        SHORT_K = 3

        def _pos_emb(L):
            t = jnp.linspace(0.0, 1.0, L)[:, None]
            t_resc = jnp.linspace(0.0, L - 1.0, L)
            w = 2.0 * math.pi * t_resc / L
            bands = (EMB_DIM - 1) // 2
            f = jnp.linspace(0.0001, bands - 1.0, bands)
            ang = f[None, :] * w[:, None]
            z = jnp.concatenate([t, jnp.cos(ang), -jnp.sin(ang)], axis=-1)
            return (z, t)

        def _filter_k(L, w0, b0, freq, w1, b1, w2, b2, w3):
            z, t = _pos_emb(L)
            h = jnp.sin(freq * (z @ w0.T + b0))
            h = jnp.sin(freq * (h @ w1.T + b1))
            h = jnp.sin(freq * (h @ w2.T + b2))
            h = h @ w3.T
            max_decay = math.log(0.01) / 0.3
            min_decay = math.log(0.01) / 1.5
            deltas = jnp.linspace(min_decay, max_decay, h.shape[-1])
            decay = jnp.exp(-t * jnp.abs(deltas)[None, :])
            return (h * decay).T

        def _fftconv(u, k, bias):
            L = u.shape[-1]
            n = 2 * L
            k_f = jnp.fft.rfft(k, n=n) / n
            u_f = jnp.fft.rfft(u, n=n)
            y = jnp.fft.irfft(u_f * k_f, n=n, norm='forward')[..., :L]
            return y + u * bias[:, None]
        key = jax.random.key(seed)
        ks = jax.random.split(key, 16)
        D = D_MODEL

        def n(k, shape, scale=0.02):
            return jax.random.normal(k, shape, dtype=jnp.float32) * scale
        return {'x': jax.random.normal(ks[0], (B, L_MAX, D), dtype=jnp.float32), 'in_proj_w': n(ks[1], (3 * D, D)), 'in_proj_b': n(ks[2], (3 * D,)), 'short_w': n(ks[3], (3 * D, 1, SHORT_K), 0.3), 'short_b': n(ks[4], (3 * D,), 0.1), 'mlp_w0': n(ks[5], (FILTER_ORDER, EMB_DIM), 0.5), 'mlp_b0': n(ks[6], (FILTER_ORDER,), 0.5), 'sin_freq': jnp.ones((1, FILTER_ORDER), dtype=jnp.float32), 'mlp_w1': n(ks[7], (FILTER_ORDER, FILTER_ORDER), 0.1), 'mlp_b1': n(ks[8], (FILTER_ORDER,), 0.1), 'mlp_w2': n(ks[9], (FILTER_ORDER, FILTER_ORDER), 0.1), 'mlp_b2': n(ks[10], (FILTER_ORDER,), 0.1), 'mlp_w3': n(ks[11], (D, FILTER_ORDER), 0.1), 'filter_bias': jax.random.normal(ks[12], (D,), dtype=jnp.float32), 'out_proj_w': n(ks[13], (D, D)), 'out_proj_b': n(ks[14], (D,))}
    _L0_attn_in = _L0_attn_setup()

    def _L0_ffn_setup():
        import jax, jax.numpy as jnp
        import numpy as np
        DIM = 512
        HID = 1408
        ZERO_POINT = 128.0

        def _qlinear(x, wq, scale):
            W = (wq.astype(jnp.float32) - ZERO_POINT) * scale[:, None]
            return jnp.einsum('bsd,hd->bsh', x, W)
        key = jax.random.key(seed)
        ks = jax.random.split(key, 7)
        B, S = (4, 512)
        sg = jax.random.uniform(ks[1], (HID,)) * (0.02 / np.sqrt(DIM)) + 0.0001
        su = jax.random.uniform(ks[3], (HID,)) * (0.02 / np.sqrt(DIM)) + 0.0001
        sd = jax.random.uniform(ks[5], (DIM,)) * (0.02 / np.sqrt(HID)) + 0.0001
        return {'x': jax.random.normal(ks[0], (B, S, DIM), dtype=jnp.float32), 'wq_gate': jax.random.randint(ks[2], (HID, DIM), 0, 64, dtype=jnp.int32), 's_gate': sg, 'wq_up': jax.random.randint(ks[4], (HID, DIM), 0, 64, dtype=jnp.int32), 's_up': su, 'wq_down': jax.random.randint(ks[6], (DIM, HID), 0, 64, dtype=jnp.int32), 's_down': sd}
    _L0_ffn_in = _L0_ffn_setup()
    _d = {'L0_attn_x': _L0_attn_in['x'], 'L0_attn_in_proj_w': _L0_attn_in['in_proj_w'], 'L0_attn_in_proj_b': _L0_attn_in['in_proj_b'], 'L0_attn_short_w': _L0_attn_in['short_w'], 'L0_attn_short_b': _L0_attn_in['short_b'], 'L0_attn_mlp_w0': _L0_attn_in['mlp_w0'], 'L0_attn_mlp_b0': _L0_attn_in['mlp_b0'], 'L0_attn_sin_freq': _L0_attn_in['sin_freq'], 'L0_attn_mlp_w1': _L0_attn_in['mlp_w1'], 'L0_attn_mlp_b1': _L0_attn_in['mlp_b1'], 'L0_attn_mlp_w2': _L0_attn_in['mlp_w2'], 'L0_attn_mlp_b2': _L0_attn_in['mlp_b2'], 'L0_attn_mlp_w3': _L0_attn_in['mlp_w3'], 'L0_attn_filter_bias': _L0_attn_in['filter_bias'], 'L0_attn_out_proj_w': _L0_attn_in['out_proj_w'], 'L0_attn_out_proj_b': _L0_attn_in['out_proj_b'], 'L0_ffn_wq_gate': _L0_ffn_in['wq_gate'], 'L0_ffn_s_gate': _L0_ffn_in['s_gate'], 'L0_ffn_wq_up': _L0_ffn_in['wq_up'], 'L0_ffn_s_up': _L0_ffn_in['s_up'], 'L0_ffn_wq_down': _L0_ffn_in['wq_down'], 'L0_ffn_s_down': _L0_ffn_in['s_down']}
    _x0 = _d['L0_attn_x']
    _d['L0_attn_x'] = jax.random.normal(jax.random.fold_in(jax.random.key(seed), 1), (8, 512, 512), dtype=_x0.dtype)
    del _x0
    return _d

def reference(L0_attn_x, L0_attn_in_proj_w, L0_attn_in_proj_b, L0_attn_short_w, L0_attn_short_b, L0_attn_mlp_w0, L0_attn_mlp_b0, L0_attn_sin_freq, L0_attn_mlp_w1, L0_attn_mlp_b1, L0_attn_mlp_w2, L0_attn_mlp_b2, L0_attn_mlp_w3, L0_attn_filter_bias, L0_attn_out_proj_w, L0_attn_out_proj_b, L0_ffn_wq_gate, L0_ffn_s_gate, L0_ffn_wq_up, L0_ffn_s_up, L0_ffn_wq_down, L0_ffn_s_down):

    def _L0_attn_ref(x, in_proj_w, in_proj_b, short_w, short_b, mlp_w0, mlp_b0, sin_freq, mlp_w1, mlp_b1, mlp_w2, mlp_b2, mlp_w3, filter_bias, out_proj_w, out_proj_b):
        import jax, jax.numpy as jnp
        import numpy as np
        import math
        B = 2
        D_MODEL = 512
        L_MAX = 1024
        FILTER_ORDER = 64
        EMB_DIM = 3
        SHORT_K = 3

        def _pos_emb(L):
            t = jnp.linspace(0.0, 1.0, L)[:, None]
            t_resc = jnp.linspace(0.0, L - 1.0, L)
            w = 2.0 * math.pi * t_resc / L
            bands = (EMB_DIM - 1) // 2
            f = jnp.linspace(0.0001, bands - 1.0, bands)
            ang = f[None, :] * w[:, None]
            z = jnp.concatenate([t, jnp.cos(ang), -jnp.sin(ang)], axis=-1)
            return (z, t)

        def _filter_k(L, w0, b0, freq, w1, b1, w2, b2, w3):
            z, t = _pos_emb(L)
            h = jnp.sin(freq * (z @ w0.T + b0))
            h = jnp.sin(freq * (h @ w1.T + b1))
            h = jnp.sin(freq * (h @ w2.T + b2))
            h = h @ w3.T
            max_decay = math.log(0.01) / 0.3
            min_decay = math.log(0.01) / 1.5
            deltas = jnp.linspace(min_decay, max_decay, h.shape[-1])
            decay = jnp.exp(-t * jnp.abs(deltas)[None, :])
            return (h * decay).T

        def _fftconv(u, k, bias):
            L = u.shape[-1]
            n = 2 * L
            k_f = jnp.fft.rfft(k, n=n) / n
            u_f = jnp.fft.rfft(u, n=n)
            y = jnp.fft.irfft(u_f * k_f, n=n, norm='forward')[..., :L]
            return y + u * bias[:, None]
        Bn, L, D = x.shape
        u = x @ in_proj_w.T + in_proj_b
        u = jnp.transpose(u, (0, 2, 1))
        uc = jax.lax.conv_general_dilated(u, short_w, window_strides=(1,), padding=[(SHORT_K - 1, SHORT_K - 1)], feature_group_count=3 * D, dimension_numbers=('NCH', 'OIH', 'NCH'))
        uc = uc[..., :L] + short_b[None, :, None]
        x0, x1, v = jnp.split(uc, 3, axis=1)
        k = _filter_k(L, mlp_w0, mlp_b0, sin_freq, mlp_w1, mlp_b1, mlp_w2, mlp_b2, mlp_w3)
        v = v * x1
        v = _fftconv(v, k, filter_bias)
        y = v * x0
        y = jnp.transpose(y, (0, 2, 1))
        return y @ out_proj_w.T + out_proj_b

    def _L0_ffn_ref(x, wq_gate, s_gate, wq_up, s_up, wq_down, s_down):
        import jax, jax.numpy as jnp
        import numpy as np
        DIM = 512
        HID = 1408
        ZERO_POINT = 128.0

        def _qlinear(x, wq, scale):
            W = (wq.astype(jnp.float32) - ZERO_POINT) * scale[:, None]
            return jnp.einsum('bsd,hd->bsh', x, W)
        gate = _qlinear(x, wq_gate, s_gate)
        gate = jax.nn.silu(gate)
        up = _qlinear(x, wq_up, s_up)
        return _qlinear(gate * up, wq_down, s_down)
    x = L0_attn_x
    x = _layernorm(x + _L0_attn_ref(x, L0_attn_in_proj_w, L0_attn_in_proj_b, L0_attn_short_w, L0_attn_short_b, L0_attn_mlp_w0, L0_attn_mlp_b0, L0_attn_sin_freq, L0_attn_mlp_w1, L0_attn_mlp_b1, L0_attn_mlp_w2, L0_attn_mlp_b2, L0_attn_mlp_w3, L0_attn_filter_bias, L0_attn_out_proj_w, L0_attn_out_proj_b), axis=-1)
    x = _layernorm(x + _L0_ffn_ref(x, L0_ffn_wq_gate, L0_ffn_s_gate, L0_ffn_wq_up, L0_ffn_s_up, L0_ffn_wq_down, L0_ffn_s_down), axis=-1)
    return x

_drawn_inputs = setup_inputs


def setup_inputs(seed=0):
    import zlib

    import numpy as np

    out = dict(_drawn_inputs(seed))
    spreads = {'L0_attn_sin_freq': (1.0, 0.6)}
    factors = {'L0_attn_in_proj_b': 8.0,
     'L0_attn_mlp_w0': 2.982,
     'L0_attn_mlp_b1': 8.0,
     'L0_attn_mlp_b2': 8.0,
     'L0_attn_filter_bias': 6.667,
     'L0_attn_out_proj_b': 3.006,
     'L0_ffn_s_gate': 5.956,
     'L0_ffn_s_up': 6.626,
     'L0_ffn_s_down': 3.072}
    for name, (base, spread) in spreads.items():
        noise = np.random.default_rng([zlib.crc32(name.encode()), seed]).standard_normal(out[name].shape)
        drawn = base * np.exp(spread * noise) if base else spread * noise
        out[name] = jnp.asarray(drawn.astype(out[name].dtype))
    for name, factor in factors.items():
        out[name] = (out[name] * factor).astype(out[name].dtype)
    return out
```

```python
from contextlib import ExitStack

import concourse.bass as bass
from concourse import mybir

P = 128
NSEQ, L, D = 8, 512, 512
HID = 1408
TB = L // P
CB = D // P
HB = HID // P
TAPS = 3
ORDER = 64
EPS = 1e-5
ZERO_POINT = 128.0
V, X1, X0 = 0, 1, 2
COLS = {V: 2, X1: 1, X0: 0}
MAGIC = 12582912.0
TWO_PI = 6.283185307179586
TWO_PI_HI = 6.28125
PI_BELOW = 3.1415925

F32 = mybir.dt.float32
F32R = mybir.dt.float32r
F16 = mybir.dt.float16
BF16 = mybir.dt.bfloat16
I32 = mybir.dt.int32
ALU = mybir.AluOpType
ACT = mybir.ActivationFunctionType


def plan(i, attn, prev, ffn, tail):
    steps = [("ip", 0, V), ("conv", 0, V), ("ip", 0, X1)] * attn
    steps += [("dn", -2, HB - 1)] * tail
    steps += [("conv", 0, X1), ("v1", 0)] * attn
    steps += [("ip", 0, X0)] * attn + [("tp", -1, 0), ("ptsplit", -1, 0)] * prev + [("conv", 0, X0)] * attn
    steps += [("tv", 0), ("vsplit", 0)] * attn
    steps += [("iv", -1, 0), ("tp", -1, 1), ("ptsplit", -1, 1), ("iv", -1, 1), ("z", -1), ("resid", -1)] * prev
    steps += [("fw", 0)] * attn
    steps += [("ln2", -2, 0), ("ln2", -2, 1), ("norm2", -2, 0), ("norm2", -2, 1)] * tail
    steps += [("prod", 0, 0), ("prod", 0, 1), ("prod", 0, 2)] * attn
    ops = [("op", -1, tb) for tb in range(TB)] * prev
    steps += ops[:2] if attn else ops
    ln1 = [("ln1", -1, 0), ("ln1", -1, 1)] * prev
    norm1 = [("norm1", -1, 0), ("norm1", -1, 1)] * prev
    x2t = [step for tb in range(TB) for step in (("x2t", -1, tb), ("x2split", -1, tb))] * ffn
    if not attn:
        steps += ln1 + norm1 + x2t
        for j in range(HB if ffn else 0):
            steps += [("gu", -1, j)] + [("dn", -1, j - 1)] * (j > 0) + [("h", -1, j)]
        return steps
    steps += [("ip", 1, V), ("conv", 1, V)] + ln1[:1] + [("ip", 1, X1), ("conv", 1, X1), ("v1", 1)] + norm1[:1]
    steps += [("ip", 1, X0), ("tp", 0, 0), ("ptsplit", 0, 0), ("conv", 1, X0)] + ops[2:] + [("tv", 1), ("vsplit", 1), ("iv", 0, 0)]
    steps += [("tp", 0, 1), ("ptsplit", 0, 1)] + ln1[1:] + [("iv", 0, 1), ("z", 0), ("fw", 1)] + norm1[1:]
    steps += [("prod", 1, 0)] + x2t + [("prod", 1, 1)]
    steps += [("gu", -1, 0)] * ffn + [("prod", 1, 2)]
    steps += [("h", -1, 0), ("gu", -1, 1), ("dn", -1, 0), ("h", -1, 1)] * ffn

    def gate_up(j):
        return [("gu", -1, j)] * ffn

    def hidden(j):
        return [("h", -1, j)] * ffn

    def downs(j):
        return [("dn", -1, j)] * ffn

    for c, (a, b, k, e, f) in ((2, (2, 3, 4, None, 5)), (3, (6, 7, 8, 9, 10))):
        steps += [("ip", c, V), ("conv", c, V)] + gate_up(a) + downs(a - 1)
        steps += [("ip", c, X1)] + hidden(a) + [("conv", c, X1), ("v1", c), ("tp", c - 1, 0), ("ptsplit", c - 1, 0)]
        steps += downs(a) + [("ip", c, X0), ("conv", c, X0)] + gate_up(b) + [("iv", c - 1, 0)] + hidden(b)
        steps += [("tp", c - 1, 1), ("ptsplit", c - 1, 1)] + downs(b) + gate_up(k) + [("iv", c - 1, 1)]
        steps += hidden(k) + [("z", c - 1)]
        if c == CB - 1 and i != NSEQ - 1:
            steps += [("xt", 0, 0), ("xsplit", 0, 0), ("xt", 0, 1), ("xsplit", 0, 1)]
            steps += downs(k) + [("xt", 0, 2), ("xsplit", 0, 2), ("xt", 0, 3), ("xsplit", 0, 3)]
        elif c == CB - 1:
            steps += downs(k)
        if c == CB - 1:
            steps += gate_up(e) + [("tv", c)] + hidden(e) + [("vsplit", c)]
        else:
            steps += [("tv", c), ("vsplit", c)] + downs(k)
        steps += [("fw", c)] + (downs(e) if e is not None else []) + [("prod", c, 0)] + gate_up(f) + [("prod", c, 1)] + hidden(f) + [("prod", c, 2)]
    return steps


PRODUCTS = [
    [(2, 2, 0), (2, 1, 1)],
    [(0, 2, 0), (0, 2, 1)],
    [(0, 2, 2), (0, 1, 3)],
]
FIRST_TO_TARGET = {(2, 2, 0), (0, 2, 0)}
STEPS_BEFORE = [[0, 2], [5, 7], [10, 13]]
SUMS_BEFORE = [[None, 0], [None, 1], [2, 3]]
PROD_STEPS, IM_SUMS = 16, 4
BANK_B_READ, BANK_A_READ = 4, 15


def build(nc, x, win, wout, wg, wu, wd, fwd, shifted, inv, decay, z_pos, w0, w1, w2, w3, net_cols, fbias,
          conv_w, conv_cols, gate_cols, up_cols, down_row, out_row, identity, out):
    ctx = ExitStack()
    with ctx:
        def sb(name, shape, dt):
            return ctx.enter_context(nc.sbuf_tensor(name, shape, dt))

        def sem(name):
            return ctx.enter_context(nc.semaphore(name))

        win_hi, win_lo = (sb(f"win_{n}", [P, CB, 3 * D], F32R) for n in ("hi", "lo"))
        wout_hi, wout_lo = (sb(f"wout_{n}", [P, CB, D], F32R) for n in ("hi", "lo"))
        wg_sb, wu_sb = (sb(f"w{n}_sb", [P, CB, HID], BF16) for n in "gu")
        wd_sb = sb("wd_sb", [P, HB, D], F32R)
        fwd_hi, fwd_lo = (sb(f"fwd_{n}", [P, 2 * P], F32R) for n in ("hi", "lo"))
        inv_hi, inv_lo = (sb(f"inv_{n}", [P, 2, P], F32R) for n in ("hi", "lo"))
        filt = sb("filt", [P, CB, TB, 2, P], F32)
        ident = sb("ident", [P, P], F32)
        down_scale = sb("down_scale", [P, D], F32)
        out_bias = sb("out_bias", [P, D], F32)
        taps = sb("taps", [P, 12, TAPS], F32)
        in_out_bias = sb("in_out_bias", [P, 2, 12], F32)
        conv_bias = sb("conv_bias", [P, TAPS, 12], F32)
        gate_scale, up_scale = (sb(f"{n}_scale", [P, HB], F32) for n in ("gate", "up"))
        net = sb("net", [ORDER, 4], F32)
        small_w = sb("small_w", [ORDER, 3, ORDER], F32)
        minus_half = sb("minus_half", [P, 2], F32)
        x_tile = sb("x_tile", [P, 2, D], F32)
        xT_hi, xT_lo = (sb(f"xT_{n}", [P, CB, L], F32R) for n in ("hi", "lo"))
        cv = [sb("conv_v", [P, L], F32), sb("conv_x1", [P, L], F32)]
        cx0 = [sb(f"conv_x0_{n}", [P, L], F32) for n in range(2)]
        vT_hi, vT_lo = (sb(f"vT_{n}", [P, TB, P], F32R) for n in ("hi", "lo"))
        by_re = sb("by_re", [P, 2 * TB, P], F32)
        by_im = sb("by_im", [P, 2 * TB, P], F32)
        tmp = [sb(f"tmp_{n}", [P, 4, P], F32) for n in range(2)]
        pT_hi, pT_lo = (sb(f"pT_{n}", [P, 4, P], F32R) for n in ("hi", "lo"))
        z_hi, z_lo = (sb(f"z_{n}", [P, CB, L], F32R) for n in ("hi", "lo"))
        x2 = sb("x2", [P, TB, D], F32)
        x2T_hi, x2T_lo = (sb(f"x2T_{n}", [P, CB, L], F16) for n in ("hi", "lo"))
        hid = sb("hid", [P, L], F32)
        res_extra = sb("res_extra", [P, D], F32)
        residual = [x_tile[:, 0, :], x_tile[:, 1, :], hid[:, :], res_extra[:, :]]
        hid_hi, hid_lo = (sb(f"hid_{n}", [P, L], F32R) for n in ("hi", "lo"))
        stats = sb("stats", [P, 2, TB, 6], F32)
        mean_gap, mean_twice, square_sum, var_eps = (
            sb(n, [P, 2, TB], F32) for n in ("mean_gap", "mean_twice", "square_sum", "var_eps"))
        rstd = sb("rstd", [P, 2, TB], F32)
        shift = sb("shift", [P, 2, TB], F32)
        down = [ctx.enter_context(nc.psum_tensor(f"down{n}", [P, D], F32)) for n in range(TB)]
        gate_ps = ctx.enter_context(nc.psum_tensor("gate_ps", [P, L], F32))
        up_ps = ctx.enter_context(nc.psum_tensor("up_ps", [P, L], F32))
        bank = [ctx.enter_context(nc.psum_tensor(f"attn{n}", [P, 512], F32)) for n in range(2)]
        proj_bank = [{V: bank[0], X1: gate_ps, X0: up_ps}] * 2 + [{V: bank[0], X1: bank[1], X0: bank[1]}] * 2
        v1t_bank = [gate_ps, gate_ps, bank[0], bank[0]]
        x2t_bank = [gate_ps, up_ps, gate_ps, up_ps]

        consts_in, taps_in, late_in = sem("consts_in"), sem("taps_in"), sem("late_in")
        decay_in = sem("decay_in")
        staged = [sem(f"staged{n}") for n in range(TB)]
        x_in = [sem(f"x_in{n}") for n in range(2)]
        res_in = [sem(f"res_in{n}") for n in range(TB)]
        stored = [sem(f"stored{n}") for n in range(TB)]
        stage_hi, stage_used, int_used = sem("stage_hi"), sem("stage_used"), sem("int_used")
        bias_step, half_set = sem("bias_step"), sem("half_set")
        net_mm, net_step, net_sin = sem("net_mm"), sem("net_step"), sem("net_sin")
        k_mm, k_done, filt_mm, filt_done = sem("k_mm"), sem("k_done"), sem("filt_mm"), sem("filt_done")
        xt_ready, ip_ready, tv_ready, fw_ready = sem("xt_ready"), sem("ip_ready"), sem("tv_ready"), sem("fw_ready")
        tp_ready, iv_ready, op_ready = sem("tp_ready"), sem("iv_ready"), sem("op_ready")
        xt_hi_done, xt_lo_done = sem("xt_hi_done"), sem("xt_lo_done")
        tap2_done, tap1_done, conv_done, v1_done = sem("tap2_done"), sem("tap1_done"), sem("conv_done"), sem("v1_done")
        vt_hi_done, vt_lo_done = sem("vt_hi_done"), sem("vt_lo_done")
        prod_step, im_sum = sem("prod_step"), sem("im_sum")
        spec_done = sem("spec_done")
        pt_hi_done, pt_lo_done = sem("pt_hi_done"), sem("pt_lo_done")
        z_done, z_hi_done, z_lo_done = sem("z_done"), sem("z_hi_done"), sem("z_lo_done")
        res_biased, ln2_scaled = sem("res_biased"), sem("ln2_scaled")
        ln_sum, ln_stats, ln_part, ln_var, ln_rstd, ln_shift, ln_done = (
            [sem(f"ln{w}_{n}") for w in (1, 2)] for n in ("sum", "stats", "part", "var", "rstd", "shift", "done"))
        x2t_ready, x2t_hi_done, x2t_lo_done = sem("x2t_ready"), sem("x2t_hi_done"), sem("x2t_lo_done")
        gate_ready, up_ready, dn_done = sem("gate_ready"), sem("up_ready"), sem("dn_done")
        silu_done, h_done, h_hi_done, h_lo_done = sem("silu_done"), sem("h_done"), sem("h_hi_done"), sem("h_lo_done")

        def f32(ap):
            return ap.bitcast(F32)

        floats = [(fwd, 2 * P, fwd_hi[:, :], fwd_lo[:, :]),
                  (inv, 2 * P, inv_hi[:, :, :].rearrange("p a b -> p (a b)"),
                   inv_lo[:, :, :].rearrange("p a b -> p (a b)"))]
        for col in (COLS[V], COLS[X1], COLS[X0]):
            for kb in range(CB):
                cs = slice(col * D, (col + 1) * D)
                floats.append((win[kb * P:(kb + 1) * P, cs], D, win_hi[:, kb, cs], win_lo[:, kb, cs]))
        for kb in range(CB):
            floats.append((wout[kb * P:(kb + 1) * P, :], D, wout_hi[:, kb, :], wout_lo[:, kb, :]))
        codes = []
        for src, dst in ((wg, wg_sb), (wu, wu_sb)):
            for kb in range(CB):
                for a in range(0, HID, D):
                    b = min(a + D, HID)
                    codes.append((src[kb * P:(kb + 1) * P, a:b], b - a, dst[:, kb, a:b]))
        for j in range(HB):
            codes.append((wd[j * P:(j + 1) * P, :], D, wd_sb[:, j, :]))
        NFLOAT, NCODE = len(floats), len(codes)

        def bodies(eng, run):
            run(0, plan(0, 1, 0, 0, 0))
            run(1, plan(1, 1, 1, 1, 0))
            with eng.Fori(2, NSEQ - 1) as i:
                run(i, plan(2, 1, 1, 1, 1))
            run(NSEQ - 1, plan(NSEQ - 1, 1, 1, 1, 1))
            run(NSEQ, plan(NSEQ, 0, 1, 1, 1))
            run(NSEQ + 1, plan(NSEQ + 1, 0, 0, 0, 1))

        block = ctx.enter_context(nc.Block())

        @block.sync
        def _(sp):
            def load_x(s, tb):
                n = s * TB + tb
                return sp.dma_start(x_tile[:, tb % 2, :], x[bass.ds(n * P, P), :] if not isinstance(n, int)
                                    else x[n * P:(n + 1) * P, :]).then_inc(x_in[tb % 2], 16)

            sp.dma_start(small_w[:, 1, :], w1).then_inc(consts_in, 16)
            sp.dma_start(small_w[:, 2, :], w2).then_inc(consts_in, 16)
            load_x(0, 0)
            load_x(0, 1)
            for n, (src, cols, *_) in enumerate(floats):
                if n >= TB:
                    sp.wait_ge(stage_used, n - TB + 1)
                sp.dma_start(x2[:, n % TB, :cols], src).then_inc(staged[n % TB], 16)
                if n == 4 or n == 5:
                    sp.wait_ge(xt_ready, n - 3)
                    load_x(0, n - 2)
            sp.wait_ge(filt_done, 2 * CB)
            sp.dma_start(down_scale[:, :], down_row).then_inc(late_in, 16)
            sp.dma_start(out_bias[:, :], out_row).then_inc(late_in, 16)
            for m, (src, cols, _) in enumerate(codes):
                n = NFLOAT + m
                if n - TB < NFLOAT:
                    sp.wait_ge(stage_used, n - TB + 1)
                else:
                    sp.wait_ge(int_used, n - TB - NFLOAT + 1)
                sp.dma_start(x2[:, n % TB, :cols].bitcast(I32), src).then_inc(staged[n % TB], 16)

            def run(i, steps):
                has = {(s[0], s[1]) for s in steps}
                if ("resid", -1) in steps:
                    load_residuals(i)
                if ("ln2", -2, 0) in steps:
                    store_outputs(i)
                if ("xt", 0) in has:
                    for tb in range(TB):
                        sp.wait_ge(xt_ready, TB * i + TB + tb - 1)
                        if ("resid", -1) in steps and tb < 2:
                            sp.wait_ge(ln_sum[0], TB * (i - 1) + tb + 1)
                        load_x(i + 1, tb)

            def load_residuals(i):
                s = i - 1
                for tb in range(TB):
                    if tb < 2:
                        if tb == 0:
                            sp.wait_ge(xt_ready, TB * NSEQ if isinstance(i, int) and i == NSEQ else TB * (i + 1))
                            if isinstance(i, int) and i == NSEQ:
                                sp.wait_ge(ln_sum[0], TB * s)
                    elif not (isinstance(i, int) and i == 1):
                        if tb == 2:
                            sp.wait_ge(h_lo_done, HB * s)
                        else:
                            sp.wait_ge(ln_sum[0], TB * s)
                    row = (s * TB + tb) * P
                    src = x[row:row + P, :] if isinstance(row, int) else x[bass.ds(row, P), :]
                    sp.dma_start(residual[tb], src).then_inc(res_in[tb], 16)

            def store_outputs(i):
                s = i - 2
                for tb in range(TB):
                    sp.wait_ge(ln_done[1], TB * s + tb + 1)
                    row = (s * TB + tb) * P
                    dst = out[row:row + P, :] if isinstance(row, int) else out[bass.ds(row, P), :]
                    sp.dma_start(dst, x2[:, tb, :]).then_inc(stored[tb], 16)

            bodies(sp, run)
            for tb in range(TB):
                sp.wait_ge(stored[tb], 16 * NSEQ)

        @block.scalar
        def _(act):
            A = nc.scalar.activation
            act.dma_start(ident[:, :], identity).then_inc(taps_in, 16)
            act.dma_start(down_scale[:3, :], z_pos).then_inc(consts_in, 16)
            act.dma_start(small_w[:3, 0, :], w0).then_inc(consts_in, 16)
            act.dma_start(net[:, :], net_cols).then_inc(consts_in, 16)
            act.dma_start(out_bias[:ORDER, :], w3).then_inc(consts_in, 16)
            act.dma_start(taps[:, :, :], conv_w).then_inc(taps_in, 16)
            act.dma_start(in_out_bias[:, :, :], conv_cols).then_inc(taps_in, 16)
            act.dma_start(gate_scale[:, :], gate_cols).then_inc(taps_in, 16)
            act.dma_start(up_scale[:, :], up_cols).then_inc(taps_in, 16)
            for d in range(TB):
                dst = (by_re if d < 2 else by_im)[:, 4 * (d % 2):4 * (d % 2) + 4, :]
                act.dma_start(dst.rearrange("p a b -> p (a b)"), decay[d * P:(d + 1) * P, :]).then_inc(decay_in, 16)
            act.dma_start(tmp[1][:1, :, :].rearrange("p a b -> p (a b)"), fbias).then_inc(decay_in, 16)
            act.dma_start(hid[:, :2 * P], fwd).then_inc(decay_in, 16)
            act.dma_start(hid[:, 2 * P:], shifted).then_inc(decay_in, 16)

            def split_stage(n):
                src, cols, hi, _ = floats[n]
                act.wait_ge(staged[n % TB], 16 * (n // TB) + 16)
                A(hi, x2[:, n % TB, :cols], ACT.Copy).then_inc(stage_hi, 1)

            def xsplit(s, tb):
                act.wait_ge(xt_ready, TB * s + tb + 1)
                src = bank[tb % 2][:, :].rearrange("p (c t) -> p c t", c=CB)
                A(xT_hi[:, :, tb * P:(tb + 1) * P], src, ACT.Copy).then_inc(xt_hi_done, 1)

            for n in range(2):
                split_stage(n)
            for tb in range(TB):
                xsplit(0, tb)
            for n in range(2, 6):
                split_stage(n)
            n = 6
            for layer in range(3):
                act.wait_ge(net_step, 6 * (layer + 1))
                A(tmp[0][:ORDER, :, :], tmp[0][:ORDER, :, :], ACT.Sin).then_inc(net_sin, 1)
                for n in range(6 + 2 * layer, 8 + 2 * layer):
                    split_stage(n)
            for n in range(12, NFLOAT):
                split_stage(n)
            for m in range(2 * CB):
                act.wait_ge(filt_mm, m + 1)
                c, pair = m // 2, m % 2
                A(filt[:, c, 2 * pair:2 * pair + 2, :, :].rearrange("p d r f -> p (d r f)"), bank[m % 2][:, :],
                  ACT.Copy).then_inc(filt_done, 1)

            def conv(n, c, t):
                q = COLS[t] * CB + c
                dst = cv[t] if t != X0 else cx0[c % 2]
                act.wait_ge(ip_ready, 3 * n + t + 1)
                if t == V and not isinstance(n, int) or t == V and n > 0:
                    act.wait_ge(tv_ready, n)
                if t == X1 and (not isinstance(n, int) or n > 0):
                    act.wait_ge(v1_done, n)
                if t == X0 and (not isinstance(n, int) or n > 1):
                    act.wait_ge(z_lo_done, n - 1)
                    act.wait_ge(z_hi_done, n - 1)
                for a, b in ((0, 1), (1, 2), (2, L)):
                    last = A(dst[:, a:b], proj_bank[c][t][:, a:b], ACT.Identity, scale=taps[:, q, 2:3],
                             bias=conv_bias[:, min(a, 2), q:q + 1])
                last.then_inc(tap2_done, 1)

            def run(i, steps):
                for kind, *at in steps:
                    if kind in ("conv", "vsplit", "ptsplit", "z"):
                        c = at[0]
                        n = CB * i + c
                    if kind == "conv":
                        conv(n, c, at[1])
                    elif kind == "vsplit":
                        act.wait_ge(tv_ready, n + 1)
                        if not isinstance(n, int) or n > 0:
                            act.wait_ge(fw_ready, 2 * n)
                        A(vT_hi[:, :, :].rearrange("p a b -> p (a b)"), v1t_bank[c][:, :], ACT.Copy).then_inc(vt_hi_done, 1)
                    elif kind == "ptsplit":
                        h = at[1]
                        act.wait_ge(tp_ready, 2 * n + h + 1)
                        if not isinstance(n, int) or 2 * n + h > 0:
                            act.wait_ge(iv_ready, 2 * n + h)
                        A(pT_hi[:, :, :].rearrange("p a b -> p (a b)"), bank[0][:, :], ACT.Copy).then_inc(pt_hi_done, 1)
                    elif kind == "z":
                        cc = c % CB
                        act.wait_ge(z_done, n + 1)
                        if not isinstance(n, int) or n >= CB:
                            act.wait_ge(op_ready, n - cc)
                        A(z_hi[:, cc, :], cx0[cc % 2][:, :], ACT.Copy).then_inc(z_hi_done, 1)
                    elif kind == "xsplit":
                        tb = at[1]
                        act.wait_ge(ip_ready, 3 * CB * (i + 1))
                        xsplit(i + 1, tb)
                    elif kind in ("norm1", "norm2"):
                        s, half, w = i + at[0], at[1], 0 if kind == "norm1" else 1
                        act.wait_ge(ln_shift[w], 2 * s + half + 1)
                        for tb in (2 * half, 2 * half + 1):
                            A(x2[:, tb, :], x2[:, tb, :], ACT.Identity, scale=rstd[:, w, tb:tb + 1],
                              bias=shift[:, w, tb:tb + 1]).then_inc(ln_done[w], 1)
                    elif kind == "x2split":
                        s, tb = i + at[0], at[1]
                        act.wait_ge(x2t_ready, TB * s + tb + 1)
                        src = x2t_bank[tb][:, :].rearrange("p (c t) -> p c t", c=CB)
                        A(x2T_hi[:, :, tb * P:(tb + 1) * P], src, ACT.Copy).then_inc(x2t_hi_done, 1)
                    elif kind == "h":
                        s, j = i + at[0], at[1]
                        m = HB * s + j
                        act.wait_ge(gate_ready, m + 1)
                        if not isinstance(m, int) or m > 0:
                            act.wait_ge(h_lo_done, m)
                        if j == 0:
                            act.wait_ge(ln_sum[0], TB * s + 3)
                        A(hid[:, :], gate_ps[:, :], ACT.Silu, scale=gate_scale[:, j:j + 1]).then_inc(silu_done, 1)
                        act.wait_ge(h_done, m + 1)
                        if not isinstance(m, int) or m > 0:
                            act.wait_ge(dn_done, m)
                        A(hid_hi[:, :], hid[:, :], ACT.Copy).then_inc(h_hi_done, 1)

            bodies(act, run)

        @block.gpsimd
        def _(pool):
            G = nc.gpsimd
            G.memset(minus_half[:, :], -0.5).then_inc(half_set, 1)

            def convert(m0, count):
                for m in range(m0, min(m0 + count, NCODE)):
                    n, (_, cols, dst) = NFLOAT + m, codes[m]
                    pool.wait_ge(staged[n % TB], 16 * (n // TB) + 16)
                    G.tensor_scalar(dst, x2[:, n % TB, :cols].bitcast(I32), -ZERO_POINT, 1.0, ALU.add, ALU.mult)\
                     .then_inc(int_used, 1)
                return count

            def run(i, steps):
                converted = 0
                for kind, *at in steps:
                    if kind not in ("v1", "prod", "resid", "z", "ln1", "ln2"):
                        continue
                    if kind in ("v1", "prod", "z"):
                        c = at[0]
                        n = CB * i + c
                    if kind == "v1":
                        pool.wait_ge(conv_done, 3 * n + 2)
                        G.tensor_tensor(cv[V][:, :], cv[V][:, :], cv[X1][:, :], ALU.mult).then_inc(v1_done, 1)
                    elif kind == "prod":
                        part = at[1]
                        for k, (j, blocks, d) in enumerate(PRODUCTS[part]):
                            if (j, blocks, d) in FIRST_TO_TARGET:
                                continue
                            rows = slice(2 * (j + d), 2 * (j + d) + 2 * blocks)
                            pool.wait_ge(prod_step, PROD_STEPS * n + STEPS_BEFORE[part][k] + 2)
                            sums = IM_SUMS * n + SUMS_BEFORE[part][k]
                            if not (isinstance(sums, int) and sums == 0):
                                pool.wait_ge(im_sum, sums)
                            G.tensor_tensor(by_im[:, rows, :], by_im[:, rows, :], tmp[1][:, :2 * blocks, :], ALU.add)\
                             .then_inc(im_sum, 1)
                        if part != 2:
                            continue
                        pool.wait_ge(prod_step, PROD_STEPS * (n + 1))
                        pool.wait_ge(im_sum, IM_SUMS * (n + 1))
                        re, im = by_re[:, :, :].rearrange("p (i r) f -> p i r f", r=2), \
                            by_im[:, :, :].rearrange("p (i r) f -> p i r f", r=2)
                        G.tensor_tensor(re[:, :, 0, :], re[:, :, 0, :], im[:, :, 1, :], ALU.subtract)
                        G.tensor_tensor(re[:, :, 1, :], re[:, :, 1, :], im[:, :, 0, :], ALU.add).then_inc(spec_done, 1)
                    elif kind == "z":
                        cc = c % CB
                        pool.wait_ge(z_hi_done, n + 1)
                        G.tensor_tensor(z_lo[:, cc, :], cx0[cc % 2][:, :], f32(z_hi[:, cc, :]), ALU.subtract)\
                         .then_inc(z_lo_done, 1)
                    elif kind == "resid":
                        s = i + at[0]
                        for tb in range(TB):
                            pool.wait_ge(res_in[tb], 16 * s + 16)
                            if isinstance(s, int) and s == 0:
                                pool.wait_ge(late_in, 32)
                            G.tensor_tensor(residual[tb], residual[tb], out_bias[:, :], ALU.add).then_inc(res_biased, 1)
                    elif kind in ("ln1", "ln2"):
                        s, half, w = i + at[0], at[1], 0 if kind == "ln1" else 1
                        pool.wait_ge(ln_var[w], 2 * s + half + 1)
                        hs = slice(2 * half, 2 * half + 2)
                        G.tensor_tensor(rstd[:, w, hs], var_eps[:, w, hs], minus_half[:, :], ALU.pow)\
                         .then_inc(ln_rstd[w], 1)
                    if isinstance(i, int) and i == 0:
                        converted += convert(converted, 4)

            bodies(pool, run)

        @block.vector
        def _(dve):
            Vv = nc.vector
            TT, STT, TS = Vv.tensor_tensor, Vv.scalar_tensor_tensor, Vv.tensor_scalar

            def split_stage(n):
                _, cols, hi, lo = floats[n]
                dve.wait_ge(stage_hi, n + 1)
                TT(lo, x2[:, n % TB, :cols], f32(hi), ALU.subtract).then_inc(stage_used, 1)

            def xsplit(s, tb):
                dve.wait_ge(xt_hi_done, TB * s + tb + 1)
                src = bank[tb % 2][:, :].rearrange("p (c t) -> p c t", c=CB)
                ts = slice(tb * P, (tb + 1) * P)
                TT(xT_lo[:, :, ts], src, f32(xT_hi[:, :, ts]), ALU.subtract).then_inc(xt_lo_done, 1)

            dve.wait_ge(taps_in, 80)
            STTb = [(0, 2, in_out_bias[:, 1, :]), (1, 1, conv_bias[:, 0, :]), (2, 0, conv_bias[:, 1, :])]
            done = 0
            for row, tap, base in STTb:
                TT(conv_bias[:, row, :], in_out_bias[:, 0, :], taps[:, :, tap], ALU.mult).then_inc(bias_step, 1)
                dve.wait_ge(bias_step, done + 1)
                TT(conv_bias[:, row, :], conv_bias[:, row, :], base, ALU.add).then_inc(bias_step, 1)
                dve.wait_ge(bias_step, done + 2)
                done += 2
            for n in range(2):
                split_stage(n)
            for tb in range(TB):
                xsplit(0, tb)
            for n in range(2, 6):
                split_stage(n)

            dve.wait_ge(consts_in, 96)
            arg = tmp[0][:ORDER, :, :]
            turns = cv[X1][:ORDER, :].rearrange("p (a b) -> p a b", a=4)
            step = 0
            for layer in range(3):
                dve.wait_ge(net_mm, layer + 1)
                src = bank[0][:ORDER, :].rearrange("p (a b) -> p a b", a=4)
                for op in (
                    lambda: TS(arg, src, net[:, layer:layer + 1], net[:, 3:4], ALU.add, ALU.mult),
                    lambda: TS(turns, arg, 1.0 / TWO_PI, MAGIC, ALU.mult, ALU.add),
                    lambda: TS(turns, turns, -MAGIC, None, ALU.add),
                    lambda: STT(out=arg, in0=turns, scalar=-TWO_PI_HI, in1=arg, op0=ALU.mult, op1=ALU.add),
                    lambda: STT(out=arg, in0=turns, scalar=TWO_PI_HI - TWO_PI, in1=arg, op0=ALU.mult, op1=ALU.add),
                    lambda: TS(arg, arg, PI_BELOW, -PI_BELOW, ALU.min, ALU.max),
                ):
                    op().then_inc(net_step, 1)
                    step += 1
                    dve.wait_ge(net_step, step)
                for n in range(6 + 2 * layer, 8 + 2 * layer):
                    split_stage(n)
            for d in range(TB):
                dve.wait_ge(k_mm, d + 1)
                if d == 0:
                    dve.wait_ge(decay_in, 16 * (TB + 3))
                src = (by_re if d < 2 else by_im)[:, 4 * (d % 2):4 * (d % 2) + 4, :]
                TT(src, bank[d % 2][:, :].rearrange("p (a b) -> p a b", a=4), src, ALU.mult).then_inc(k_done, 1)
            dve.wait_ge(k_done, 1)
            TT(by_re[:1, :4, :], by_re[:1, :4, :], tmp[1][:1, :, :], ALU.add).then_inc(k_done, 1)
            for n in range(12, NFLOAT):
                split_stage(n)

            def products(n, c, part, seq, has_tail):
                if part == 0:
                    dve.wait_ge(fw_ready, 2 * n + 2)
                    if isinstance(n, int) and n == 0:
                        dve.wait_ge(filt_done, 2 * CB)
                    else:
                        dve.wait_ge(tp_ready, 2 * n)
                        dve.wait_ge(spec_done, n)
                if part == 0 and c == 0 and has_tail:
                    dve.wait_ge(ln_sum[1], TB * (seq - 1))
                for k, (j, blocks, d) in enumerate(PRODUCTS[part]):
                    u = bank[1 - j // 2][:, :2 * P * blocks].rearrange("p (a f) -> p a f", f=P)
                    rows = slice(2 * (j + d), 2 * (j + d) + 2 * blocks)
                    base = PROD_STEPS * n + STEPS_BEFORE[part][k]
                    re_k, im_k = (filt[:, c, d, r:r + 1, :].to_broadcast([P, 2 * blocks, P]) for r in range(2))
                    if (j, blocks, d) in FIRST_TO_TARGET:
                        TT(by_re[:, rows, :], u, re_k, ALU.mult).then_inc(prod_step, 1)
                        TT(by_im[:, rows, :], u, im_k, ALU.mult).then_inc(prod_step, 1)
                    else:
                        dve.wait_ge(prod_step, base)
                        TT(tmp[0][:, :2 * blocks, :], u, re_k, ALU.mult).then_inc(prod_step, 1)
                        sums = IM_SUMS * n + SUMS_BEFORE[part][k]
                        if not (isinstance(sums, int) and sums == 0):
                            dve.wait_ge(im_sum, sums)
                        TT(tmp[1][:, :2 * blocks, :], u, im_k, ALU.mult).then_inc(prod_step, 1)
                        dve.wait_ge(prod_step, base + 1)
                        TT(by_re[:, rows, :], by_re[:, rows, :], tmp[0][:, :2 * blocks, :], ALU.add)\
                            .then_inc(prod_step, 1)

            def run(i, steps):
                for kind, *at in steps:
                    if kind in ("conv", "vsplit", "ptsplit", "z", "prod"):
                        c = at[0]
                        n = CB * i + c
                    if kind == "conv":
                        t = at[1]
                        q = COLS[t] * CB + c
                        dst, src = cv[t] if t != X0 else cx0[c % 2], proj_bank[c][t]
                        dve.wait_ge(tap2_done, 3 * n + t + 1)
                        STT(out=dst[:, 1:], in0=src[:, :L - 1], scalar=taps[:, q, 1:2], in1=dst[:, 1:],
                            op0=ALU.mult, op1=ALU.add).then_inc(tap1_done, 1)
                        dve.wait_ge(tap1_done, 3 * n + t + 1)
                        STT(out=dst[:, 2:], in0=src[:, :L - 2], scalar=taps[:, q, 0:1], in1=dst[:, 2:],
                            op0=ALU.mult, op1=ALU.add).then_inc(conv_done, 1)
                    elif kind == "vsplit":
                        dve.wait_ge(vt_hi_done, n + 1)
                        TT(vT_lo[:, :, :].rearrange("p a b -> p (a b)"), v1t_bank[c][:, :],
                           f32(vT_hi[:, :, :]).rearrange("p a b -> p (a b)"), ALU.subtract).then_inc(vt_lo_done, 1)
                    elif kind == "prod":
                        products(n, c, at[1], i, ("ln2", -2, 0) in steps)
                    elif kind == "ptsplit":
                        h = at[1]
                        dve.wait_ge(pt_hi_done, 2 * n + h + 1)
                        TT(pT_lo[:, :, :].rearrange("p a b -> p (a b)"), bank[0][:, :],
                           f32(pT_hi[:, :, :]).rearrange("p a b -> p (a b)"), ALU.subtract).then_inc(pt_lo_done, 1)
                    elif kind == "z":
                        dve.wait_ge(iv_ready, 2 * n + 2)
                        dve.wait_ge(conv_done, 3 * n + 3)
                        y = cx0[c % 2]
                        TT(y[:, :], bank[1][:, :], y[:, :], ALU.mult).then_inc(z_done, 1)
                    elif kind == "xsplit":
                        xsplit(i + 1, at[1])
                    elif kind == "ln1":
                        s, half = i + at[0], at[1]
                        for tb in (2 * half, 2 * half + 1):
                            dve.wait_ge(op_ready, TB * s + tb + 1)
                            dve.wait_ge(res_biased, TB * s + tb + 1)
                            if isinstance(s, int) and s == 0:
                                dve.wait_ge(int_used, NCODE)
                            else:
                                dve.wait_ge(stored[tb], 16 * s)
                            TT(x2[:, tb, :], down[tb][:, :], residual[tb], ALU.add).then_inc(ln_sum[0], 1)
                        moments(0, s, half)
                    elif kind == "ln2":
                        s, half = i + at[0], at[1]
                        if half == 0:
                            dve.wait_ge(dn_done, HB * (s + 1))
                            if isinstance(s, int) and s == 0:
                                dve.wait_ge(late_in, 32)
                            if not (isinstance(i, int) and i > NSEQ):
                                dve.wait_ge(prod_step, PROD_STEPS * CB * i)
                                dve.wait_ge(im_sum, IM_SUMS * CB * i)
                        else:
                            dve.wait_ge(ln_sum[1], TB * s + 2)
                        ts = [t[:, :, :].rearrange("p a b -> p (a b)") for t in tmp]
                        for k, tb in enumerate((2 * half, 2 * half + 1)):
                            TT(ts[k], down[tb][:, :], down_scale[:, :], ALU.mult).then_inc(ln2_scaled, 1)
                        for k, tb in enumerate((2 * half, 2 * half + 1)):
                            dve.wait_ge(ln2_scaled, TB * s + tb + 1)
                            TT(x2[:, tb, :], x2[:, tb, :], ts[k], ALU.add).then_inc(ln_sum[1], 1)
                        moments(1, s, half)
                    elif kind in ("norm1", "norm2"):
                        s, half, w = i + at[0], at[1], 0 if kind == "norm1" else 1
                        hs = slice(2 * half, 2 * half + 2)
                        dve.wait_ge(ln_rstd[w], 2 * s + half + 1)
                        STT(out=shift[:, w, hs], in0=mean_twice[:, w, hs], scalar=-0.5, in1=rstd[:, w, hs],
                            op0=ALU.mult, op1=ALU.mult).then_inc(ln_shift[w], 1)
                    elif kind == "x2split":
                        s, tb = i + at[0], at[1]
                        dve.wait_ge(x2t_hi_done, TB * s + tb + 1)
                        src = x2t_bank[tb][:, :].rearrange("p (c t) -> p c t", c=CB)
                        ts = slice(tb * P, (tb + 1) * P)
                        TT(x2T_lo[:, :, ts], src, x2T_hi[:, :, ts], ALU.subtract).then_inc(x2t_lo_done, 1)
                    elif kind == "h":
                        s, j = i + at[0], at[1]
                        m = HB * s + j
                        dve.wait_ge(silu_done, m + 1)
                        dve.wait_ge(up_ready, m + 1)
                        STT(out=hid[:, :], in0=up_ps[:, :], scalar=up_scale[:, j:j + 1], in1=hid[:, :],
                            op0=ALU.mult, op1=ALU.mult).then_inc(h_done, 1)
                        dve.wait_ge(h_hi_done, m + 1)
                        TT(hid_lo[:, :], hid[:, :], f32(hid_hi[:, :]), ALU.subtract).then_inc(h_lo_done, 1)

            def moments(w, s, half):
                tbs = (2 * half, 2 * half + 1)
                for tb in tbs:
                    dve.wait_ge(ln_sum[w], TB * s + tb + 1)
                    Vv.bn_stats(stats[:, w, tb, :], x2[:, tb, :]).then_inc(ln_stats[w], 1)
                hs = slice(2 * half, 2 * half + 2)
                even, odd = stats[:, w, hs, 0:3], stats[:, w, hs, 3:6]
                done = 5 * (2 * s + half)
                dve.wait_ge(ln_stats[w], TB * s + 2 * half + 2)
                TT(mean_gap[:, w, hs], even[:, :, 1], odd[:, :, 1], ALU.subtract).then_inc(ln_part[w], 1)
                TT(mean_twice[:, w, hs], even[:, :, 1], odd[:, :, 1], ALU.add).then_inc(ln_part[w], 1)
                TT(square_sum[:, w, hs], even[:, :, 2], odd[:, :, 2], ALU.add).then_inc(ln_part[w], 1)
                dve.wait_ge(ln_part[w], done + 1)
                STT(out=mean_gap[:, w, hs], in0=mean_gap[:, w, hs], scalar=0.25, in1=mean_gap[:, w, hs],
                    op0=ALU.mult, op1=ALU.mult).then_inc(ln_part[w], 1)
                dve.wait_ge(ln_part[w], done + 3)
                TS(square_sum[:, w, hs], square_sum[:, w, hs], 1.0 / D, EPS, ALU.mult, ALU.add).then_inc(ln_part[w], 1)
                dve.wait_ge(ln_part[w], done + 5)
                TT(var_eps[:, w, hs], square_sum[:, w, hs], mean_gap[:, w, hs], ALU.add).then_inc(ln_var[w], 1)

            bodies(dve, run)

        @block.tensor
        def _(pe):
            mm = nc.tensor.matmul

            def three(out_ap, terms):
                last, n = None, len(terms)
                for k, (ah, al, bh, bl) in enumerate(terms):
                    mm(out_ap, ah, bh, start=k == 0, stop=False)
                    mm(out_ap, ah, bl, start=False, stop=False)
                    last = mm(out_ap, al, bh, start=False, stop=k == n - 1)
                return last

            def transpose_x(s, tb):
                pe.wait_ge(x_in[tb % 2], 16 * (2 * s + tb // 2) + 16)
                for c in range(CB):
                    last = nc.tensor.transpose(bank[tb % 2][:, c * P:(c + 1) * P], x_tile[:, tb % 2, c * P:(c + 1) * P],
                                               ident[:, :])
                last.then_inc(xt_ready, 1)

            pe.wait_ge(taps_in, 80)
            for tb in range(TB):
                if tb >= 2:
                    pe.wait_ge(xt_lo_done, tb - 1)
                transpose_x(0, tb)
            pe.wait_ge(consts_in, 96)
            pe.wait_ge(xt_lo_done, TB)
            for layer in range(3):
                rhs = down_scale[:3, :] if layer == 0 else tmp[0][:ORDER, :, :].rearrange("p a b -> p (a b)")
                lhsT = small_w[:3, 0, :] if layer == 0 else small_w[:, layer, :]
                if layer:
                    pe.wait_ge(net_sin, layer)
                mm(bank[0][:ORDER, :], lhsT, rhs, start=True, stop=True).then_inc(net_mm, 1)
            pe.wait_ge(net_sin, 3)
            for d in range(TB):
                if d >= 2:
                    pe.wait_ge(k_done, d - 1)
                mm(bank[d % 2][:, :], tmp[0][:ORDER, d, :], out_bias[:ORDER, :], start=True, stop=True).then_inc(k_mm, 1)
            pe.wait_ge(k_done, TB + 1)
            pe.wait_ge(decay_in, 16 * (TB + 3))
            for m in range(2 * CB):
                c, pair = m // 2, m % 2
                if m >= 2:
                    pe.wait_ge(filt_done, m - 1)
                for d in (2 * pair, 2 * pair + 1):
                    def k_of(e):
                        return (by_re if e < 2 else by_im)[:, 4 * (e % 2) + c, :]
                    dst = bank[m % 2][:, (d % 2) * 2 * P:(d % 2 + 1) * 2 * P]
                    last = mm(dst, k_of(d), hid[:, :2 * P], start=True, stop=d == 0)
                    if d:
                        last = mm(dst, k_of(d - 1), hid[:, 2 * P:], start=False, stop=True)
                last.then_inc(filt_mm, 1)

            def run(i, steps):
                attn = any(s[0] == "ip" for s in steps)
                for kind, *at in steps:
                    if kind in ("ip", "tv", "fw", "tp", "iv"):
                        c = at[0]
                        n = CB * i + c
                        first = isinstance(n, int) and n == 0
                    if kind == "ip":
                        t = at[1]
                        if t == V and first:
                            pe.wait_ge(stage_used, 6)
                            pe.wait_ge(filt_done, 2 * CB)
                        elif t == V:
                            if c == 0:
                                pe.wait_ge(xt_lo_done, TB * (i + 1))
                            pe.wait_ge(prod_step, PROD_STEPS * (n - 1) + BANK_B_READ)
                        elif t == X1:
                            if first:
                                pe.wait_ge(stage_used, 10)
                            elif c >= 2:
                                pe.wait_ge(prod_step, PROD_STEPS * (n - 1) + BANK_A_READ)
                            elif c == 1:
                                pe.wait_ge(conv_done, 3 * n)
                                pe.wait_ge(vt_lo_done, n)
                            elif not (isinstance(i, int) and i == 1):
                                pe.wait_ge(h_done, HB * (i - 1))
                        else:
                            if first:
                                pe.wait_ge(stage_used, 14)
                            if c >= 2:
                                pe.wait_ge(conv_done, 3 * n + 2)
                        cs = slice(COLS[t] * D + c * P, COLS[t] * D + (c + 1) * P)
                        three(proj_bank[c][t][:, :], [(win_hi[:, kb, cs], win_lo[:, kb, cs], xT_hi[:, kb, :], xT_lo[:, kb, :])
                                                   for kb in range(CB)]).then_inc(ip_ready, 1)
                    elif kind == "tv":
                        pe.wait_ge(v1_done, n + 1)
                        if c >= 2:
                            pe.wait_ge(pt_lo_done, 2 * n)
                        if c == CB - 1 and ("xt", 0, 2) in steps:
                            pe.wait_ge(xt_lo_done, TB * (i + 1) + 3)
                        for j in range(TB):
                            last = nc.tensor.transpose(v1t_bank[c][:, j * P:(j + 1) * P], cv[V][:, j * P:(j + 1) * P],
                                                       ident[:, :])
                        last.then_inc(tv_ready, 1)
                    elif kind == "fw":
                        pe.wait_ge(vt_lo_done, n + 1)
                        if not first:
                            pe.wait_ge(z_done, n)
                            pe.wait_ge(pt_lo_done, 2 * n)
                        else:
                            pe.wait_ge(conv_done, 3)
                        if c == CB - 1 and ("xt", 0, 3) in steps:
                            pe.wait_ge(xt_lo_done, TB * (i + 1) + 4)
                        for j in range(TB):
                            dst = bank[1 - j // 2][:, (j % 2) * 2 * P:(j % 2 + 1) * 2 * P]
                            last = three(dst, [(vT_hi[:, j, :], vT_lo[:, j, :], fwd_hi[:, :], fwd_lo[:, :])])
                            if j % 2:
                                last.then_inc(fw_ready, 1)
                    elif kind == "tp":
                        h = at[1]
                        if h == 0:
                            pe.wait_ge(spec_done, n + 1)
                            if attn:
                                pe.wait_ge(conv_done, 3 * (n + 1) + 1)
                            else:
                                pe.wait_ge(prod_step, PROD_STEPS * (n + 1))
                        else:
                            pe.wait_ge(pt_lo_done, 2 * n + 1)
                        for k in range(4):
                            last = nc.tensor.transpose(bank[0][:, k * P:(k + 1) * P], by_re[:, 4 * h + k, :], ident[:, :])
                        last.then_inc(tp_ready, 1)
                    elif kind == "iv":
                        h = at[1]
                        pe.wait_ge(pt_lo_done, 2 * n + h + 1)
                        if h == 0 and c >= 1:
                            pe.wait_ge(conv_done, 3 * (n + 1) + 3)
                        for ii in range(2):
                            dst = bank[1][:, (2 * h + ii) * P:(2 * h + ii + 1) * P]
                            last = three(dst, [(pT_hi[:, 2 * ii + r, :], pT_lo[:, 2 * ii + r, :], inv_hi[:, r, :],
                                                inv_lo[:, r, :]) for r in range(2)])
                        last.then_inc(iv_ready, 1)
                    elif kind == "xt":
                        tb = at[1]
                        if tb == 0:
                            pe.wait_ge(pt_lo_done, 2 * (CB * i + CB - 1))
                        elif tb == 1:
                            pe.wait_ge(z_done, CB * i + CB - 1)
                        else:
                            pe.wait_ge(xt_lo_done, TB * (i + 1) + tb - 1)
                        transpose_x(i + 1, tb)
                    elif kind == "op":
                        s, tb = i + at[0], at[1]
                        if tb == 0:
                            pe.wait_ge(z_lo_done, CB * (s + 1))
                            if isinstance(s, int) and s == 0:
                                pe.wait_ge(stage_used, NFLOAT)
                        if not (isinstance(s, int) and s == 0):
                            pe.wait_ge(ln2_scaled, TB * (s - 1) + tb + 1)
                        ts = slice(tb * P, (tb + 1) * P)
                        three(down[tb][:, :], [(z_hi[:, c, ts], z_lo[:, c, ts], wout_hi[:, c, :], wout_lo[:, c, :])
                                               for c in range(CB)]).then_inc(op_ready, 1)
                    elif kind == "x2t":
                        s, tb = i + at[0], at[1]
                        pe.wait_ge(ln_done[0], TB * s + tb + 1)
                        if tb >= 2:
                            pe.wait_ge(x2t_lo_done, TB * s + tb - 1)
                        elif attn:
                            pe.wait_ge(conv_done, 3 * (CB * i + 1) + 3)
                            pe.wait_ge(vt_lo_done, CB * i + 2)
                        else:
                            pe.wait_ge(h_done, HB * s)
                        for c in range(CB):
                            last = nc.tensor.transpose(x2t_bank[tb][:, c * P:(c + 1) * P], x2[:, tb, c * P:(c + 1) * P],
                                                       ident[:, :])
                        last.then_inc(x2t_ready, 1)
                    elif kind == "gu":
                        s, j = i + at[0], at[1]
                        m = HB * s + j
                        js = slice(j * P, (j + 1) * P)
                        if j == 0:
                            pe.wait_ge(x2t_lo_done, TB * (s + 1))
                            if isinstance(s, int) and s == 0:
                                pe.wait_ge(int_used, NCODE)
                        if j > 0:
                            pe.wait_ge(silu_done, m)
                        for k in range(CB):
                            mm(gate_ps[:, :], wg_sb[:, k, js], x2T_hi[:, k, :], start=k == 0, stop=False)
                            last = mm(gate_ps[:, :], wg_sb[:, k, js], x2T_lo[:, k, :], start=False, stop=k == CB - 1)
                        last.then_inc(gate_ready, 1)
                        if j > 0:
                            pe.wait_ge(h_done, m)
                        for k in range(CB):
                            mm(up_ps[:, :], wu_sb[:, k, js], x2T_hi[:, k, :], start=k == 0, stop=False)
                            last = mm(up_ps[:, :], wu_sb[:, k, js], x2T_lo[:, k, :], start=False, stop=k == CB - 1)
                        last.then_inc(up_ready, 1)
                    elif kind == "dn":
                        s, j = i + at[0], at[1]
                        m = HB * s + j
                        pe.wait_ge(h_lo_done, m + 1)
                        if j == 0:
                            pe.wait_ge(ln_sum[0], TB * (s + 1))
                        for tb in range(TB):
                            ts = slice(tb * P, (tb + 1) * P)
                            mm(down[tb][:, :], hid_hi[:, ts], wd_sb[:, j, :], start=j == 0, stop=False)
                            last = mm(down[tb][:, :], hid_lo[:, ts], wd_sb[:, j, :], start=False, stop=j == HB - 1)
                        last.then_inc(dn_done, 1)

            bodies(pe, run)


def shape_constants():
    import numpy as np
    t = np.arange(P)[:, None]
    odd = (2 * np.arange(P)[None, :] + 1)
    angle = np.pi * t * odd / (2 * P)
    cos, sin = np.cos(angle), np.sin(angle)
    sign = np.where(np.arange(P) % 2 == 0, 1.0, -1.0)[None, :]
    fwd = np.concatenate([cos, -sin], axis=1)
    shifted = np.concatenate([sign * sin, sign * cos], axis=1)
    inv = np.concatenate([cos.T / P, -sin.T / P], axis=1)
    pos = np.linspace(0.0, 1.0, L)
    w = 2.0 * np.pi * np.arange(L) / L
    z_pos = np.stack([pos, np.cos(1e-4 * w), -np.sin(1e-4 * w)])
    deltas = np.abs(np.linspace(np.log(0.01) / 1.5, np.log(0.01) / 0.3, D))
    decay = np.exp(-pos[:, None] * deltas[None, :])
    return {k: np.ascontiguousarray(v, dtype=np.float32) for k, v in
            dict(fwd=fwd, shifted=shifted, inv=inv, decay=decay, z_pos=z_pos, identity=np.eye(P)).items()}


def layouts(inputs):
    import numpy as np
    a = {k.removeprefix("L0_"): np.asarray(v) for k, v in inputs.items()}

    def columns(v, n):
        return v.reshape(n, P).T

    out = {
        "x": a["attn_x"].reshape(NSEQ * L, D),
        "win": a["attn_in_proj_w"].T, "wout": a["attn_out_proj_w"].T,
        "wg": a["ffn_wq_gate"].T, "wu": a["ffn_wq_up"].T, "wd": a["ffn_wq_down"].T,
        "w0": a["attn_mlp_w0"].T, "w1": a["attn_mlp_w1"].T, "w2": a["attn_mlp_w2"].T, "w3": a["attn_mlp_w3"].T,
        "net_cols": np.stack([a["attn_mlp_b0"], a["attn_mlp_b1"], a["attn_mlp_b2"], a["attn_sin_freq"][0]], axis=1),
        "fbias": a["attn_filter_bias"][None, :],
        "conv_w": a["attn_short_w"].reshape(12, P, TAPS).transpose(1, 0, 2),
        "conv_cols": np.stack([columns(a["attn_in_proj_b"], 12), columns(a["attn_short_b"], 12)], axis=1),
        "gate_cols": columns(a["ffn_s_gate"], HB), "up_cols": columns(a["ffn_s_up"], HB),
        "down_row": np.broadcast_to(a["ffn_s_down"], (P, D)), "out_row": np.broadcast_to(a["attn_out_proj_b"], (P, D)),
    }
    return {k: np.ascontiguousarray(v) for k, v in out.items()}


ORDER_OF_ARGUMENTS = ["x", "win", "wout", "wg", "wu", "wd", "fwd", "shifted", "inv", "decay", "z_pos", "w0", "w1", "w2",
                      "w3", "net_cols", "fbias", "conv_w", "conv_cols", "gate_cols", "up_cols", "down_row", "out_row",
                      "identity"]


def kernel(**inputs):
    import concourse.bacc as _bacc
    from concourse import mybir as _mybir
    from concourse.bass_utils import run_bass_kernel_spmd as _run

    arrays = {**shape_constants(), **layouts(inputs)}
    nc = _bacc.Bacc("TRN2", target_bir_lowering=False, num_devices=1, dynamic_dma_scratch_size=1024)
    args = [nc.dram_tensor(f"in_{n}", arrays[n].shape, _mybir.dt.from_np(arrays[n].dtype), kind="ExternalInput").ap()
            for n in ORDER_OF_ARGUMENTS]
    out = nc.dram_tensor("out", (NSEQ * L, D), _mybir.dt.float32, kind="ExternalOutput").ap()
    build(nc, *args, out)
    r = _run(nc, [{f"in_{n}": arrays[n] for n in ORDER_OF_ARGUMENTS}], core_ids=[0])
    return r.results[0]["out"].reshape(NSEQ, L, D)
```
